# Optimizing a Trainium2 kernel written in Bass

```python
import numpy as np
import jax
import jax.numpy as jnp

def _softmax(x, axis=-1):
    return jax.nn.softmax(x, axis=axis)

def _gelu(x):
    return jax.nn.gelu(x, approximate=True)

def _silu(x):
    return jax.nn.silu(x)

def _sigmoid(x):
    return jax.nn.sigmoid(x)

def _layernorm(x, axis=-1, eps=1e-05):
    m = jnp.mean(x, axis=axis, keepdims=True)
    v = jnp.var(x, axis=axis, keepdims=True)
    return (x - m) / jnp.sqrt(v + eps)

def _scatter_add(tgt, idx, src, axis=0):
    return tgt.at[idx].add(src)

def _segment_sum(src, seg, n):
    return jax.ops.segment_sum(src, seg, n)
kernel_name = 'mk_cond_resid_d1_seqx_r2_babfcd'

def setup_inputs(seed: int=0):
    np.random.seed(seed)
    _w = jnp.asarray

    def _rec_inputs():
        import jax
        import jax.numpy as jnp
        _rk = jax.random.key(seed)
        x = 4.136e-05 + 0.9999 * jax.random.normal(jax.random.fold_in(_rk, 1), (128, 128, 512), jnp.float32)
        _lenS = 128 - jax.random.randint(jax.random.fold_in(_rk, 7), (128,), 0, max(1, 128 // 4) + 1, jnp.int32)
        _lenS2 = 128 - jax.random.randint(jax.random.fold_in(_rk, 8), (128,), 0, max(1, 128 // 4) + 1, jnp.int32)
        cond_1024 = -0.00499425 + 1.0058 * jax.random.normal(jax.random.fold_in(_rk, 11), (128, 512), jnp.float32)
        return (x, cond_1024)
    x, cond_1024 = _rec_inputs()

    def _L0_cond_setup():
        import jax, jax.numpy as jnp
        import numpy as np
        B, N, D, C = (32, 128, 512, 512)
        key = jax.random.key(seed)
        k1, k2, k3, k4 = jax.random.split(key, 4)
        scale = 1.0 / np.sqrt(D)
        return {'encoded_utterance': jax.random.normal(k1, (B, D), dtype=jnp.float32), 'element_embeddings': jax.random.normal(k2, (B, N, D), dtype=jnp.float32), 'weight_matrix': jax.random.normal(k3, (2 * D, C), dtype=jnp.float32) * scale, 'W_proj': jax.random.normal(k4, (D, D), dtype=jnp.float32) * scale, 'b_proj': jnp.zeros((D,), dtype=jnp.float32)}
    _L0_cond_all = _L0_cond_setup()
    _L0_cond_in = {k: v for k, v in _L0_cond_all.items() if k in ('weight_matrix', 'W_proj', 'b_proj')}
    del _L0_cond_all
    return {'x': x, 'cond_1024': cond_1024, 'L0_cond_weight_matrix': _L0_cond_in['weight_matrix'], 'L0_cond_W_proj': _L0_cond_in['W_proj'], 'L0_cond_b_proj': _L0_cond_in['b_proj']}

def reference(x, cond_1024, L0_cond_weight_matrix, L0_cond_W_proj, L0_cond_b_proj):
    import jax
    import jax.numpy as jnp

    def _L0_cond_ref(encoded_utterance, element_embeddings, weight_matrix, W_proj, b_proj):
        import jax, jax.numpy as jnp
        import numpy as np
        B, N, D, C = (32, 128, 512, 512)
        u = jax.nn.gelu(encoded_utterance @ W_proj + b_proj, approximate=False)
        W_u, W_e = (weight_matrix[:D], weight_matrix[D:])
        logits = (u @ W_u)[:, None, :] + jnp.einsum('bnd,dc->bnc', element_embeddings, W_e)
        return logits
    x = x + _L0_cond_ref(cond_1024, x, L0_cond_weight_matrix, L0_cond_W_proj, L0_cond_b_proj)
    return x

_drawn_inputs = setup_inputs


def setup_inputs(seed=0):
    import zlib

    import numpy as np

    out = dict(_drawn_inputs(seed))
    spreads = {'L0_cond_b_proj': (0.0, 0.1)}
    factors = {}
    for name, (base, spread) in spreads.items():
        noise = np.random.default_rng([zlib.crc32(name.encode()), seed]).standard_normal(out[name].shape)
        drawn = base * np.exp(spread * noise) if base else spread * noise
        out[name] = jnp.asarray(drawn.astype(out[name].dtype))
    for name, factor in factors.items():
        out[name] = (out[name] * factor).astype(out[name].dtype)
    return out
```

```python
from contextlib import ExitStack

import concourse.bass as bass
from concourse import mybir

F32 = mybir.dt.float32
F32R = mybir.dt.float32r
ALU = mybir.AluOpType
ACT = mybir.ActivationFunctionType

P = 128
Q = 32
NQ = P // Q
TILES_PER_CHUNK = 2
CHUNKS_PER_GROUP = 4
N_RAW = 2
N_SPLIT = 4
N_BANKS = 4
N_STORE = 4
LEAD = 3


def build_cond_residual(nc, x, cond, weight_matrix, w_proj, b_proj, out):
    B, N, D = x.shape
    C = weight_matrix.shape[1]
    assert B == P and D == C == 4 * P
    NJ = D // P
    T = TILES_PER_CHUNK
    G = CHUNKS_PER_GROUP * T
    CHUNKS = N // T
    PER_ITER = N_RAW * CHUNKS_PER_GROUP
    ITERS = CHUNKS // PER_ITER
    NM = B // Q
    assert PER_ITER % N_SPLIT == 0 and PER_ITER % N_BANKS == 0 and PER_ITER % (2 * N_STORE) == 0

    w_e_dram = weight_matrix[D:2 * D, :].rearrange("(q j k) c -> q k j c", q=NQ, j=NJ)
    w_proj_dram = w_proj.rearrange("(q j k) c -> q k j c", q=NQ, j=NJ)
    w_u_dram = weight_matrix[0:D, :].rearrange("(p e) c -> p e c", e=NJ)
    b_proj_dram = b_proj.rearrange("(p e) -> p e", e=NJ)
    cond_dram = cond.rearrange("(m i) (q w) -> q i m w", m=NM, q=NQ)
    x_dram = x.rearrange("(m i) n (q w) -> q m i n w", m=NM, q=NQ)

    with ExitStack() as ctx:
        def sb(name, shape, dt=F32):
            return ctx.enter_context(nc.sbuf_tensor(name, shape, dt))

        def sem(name):
            return ctx.enter_context(nc.semaphore(name))

        x_raw = [sb(f"x_raw{s}", [P, NM, G, P]) for s in range(N_RAW)]
        x_t = [sb(f"x_t{s}", [P, T, NJ, P]) for s in range(N_SPLIT)]
        x_hi = [sb(f"x_hi{s}", [P, T, NJ, P], F32R) for s in range(N_SPLIT)]
        x_lo = [sb(f"x_lo{s}", [P, T, NJ, P], F32R) for s in range(N_SPLIT)]
        y = [sb(f"y{s}", [P, 2, T, C]) for s in range(N_STORE)]
        w_e = sb("w_e", [P, NJ * C + C])
        w_hi = sb("w_hi", [P, NJ, C], F32R)
        w_lo = sb("w_lo", [P, NJ, C], F32R)
        w_proj_sb = sb("w_proj_sb", [P, NJ, C])
        w_u = sb("w_u", [P, NJ, C])
        b_proj_sb = sb("b_proj_sb", [P, NJ])
        cond_raw = sb("cond_raw", [P, NM, P])
        cond_t = sb("cond_t", [P, NJ, B])
        u_t = sb("u_t", [P, NJ, B])
        bias = sb("bias", [P, T, C])
        ident = sb("ident", [P, P])

        banks = [ctx.enter_context(nc.psum_tensor(f"banks{s}", [P, T, C], F32)) for s in range(N_BANKS)]
        h_psum = banks[N_BANKS - 2][:, 0, :].rearrange("p (e b) -> p e b", e=NJ)
        bias_psum = banks[N_BANKS - 1][:, 0, :]

        cond_loaded = sem("cond_loaded")
        w_proj_loaded = sem("w_proj_loaded")
        b_proj_loaded = sem("b_proj_loaded")
        w_e_loaded = sem("w_e_loaded")
        w_u_loaded = sem("w_u_loaded")
        first_x_loaded = sem("first_x_loaded")
        x_loaded = [sem(f"x_loaded{s}") for s in range(N_RAW)]
        ident_zeroed = sem("ident_zeroed")
        ident_ready = sem("ident_ready")
        cond_turned = sem("cond_turned")
        h_ready = sem("h_ready")
        u_ready = sem("u_ready")
        bias_summed = sem("bias_summed")
        bias_ready = sem("bias_ready")
        w_diag_ready = sem("w_diag_ready")
        w_hi_ready = sem("w_hi_ready")
        w_lo_ready = sem("w_lo_ready")
        turned = sem("turned")
        hi_ready = sem("hi_ready")
        lo_ready = sem("lo_ready")
        multiplied = sem("multiplied")
        evacuated = sem("evacuated")
        stored = [sem(f"stored{s}") for s in range(N_STORE)]

        block = ctx.enter_context(nc.Block())

        LOADS = NQ * NM * 16

        @block.sync
        def _(sp):
            def load_x(slot, n, n_in_slot, count, loaded):
                for m in range(NM):
                    for q in range(NQ):
                        sp.dma_start(x_raw[slot][Q * q:Q * (q + 1), m, n_in_slot:n_in_slot + count, :],
                                     x_dram[q, m, :, bass.ds(n, count), :]).then_inc(loaded, 16)

            def store(slot, n):
                sp.dma_start(out[:, bass.ds(n, 2 * T), :],
                             y[slot][:, :, :, :].rearrange("p a t c -> p (a t) c")).then_inc(stored[slot], 16)

            for q in range(NQ):
                sp.dma_start(cond_raw[Q * q:Q * (q + 1), :, :], cond_dram[q]).then_inc(cond_loaded, 16)
            for q in range(NQ):
                sp.dma_start(w_proj_sb[Q * q:Q * (q + 1), :, :], w_proj_dram[q]).then_inc(w_proj_loaded, 16)
            load_x(0, 0, 0, T, first_x_loaded)
            load_x(0, T, T, G - T, x_loaded[0])
            sp.dma_start(w_u[:, :, :], w_u_dram).then_inc(w_u_loaded, 16)
            load_x(1, G, 0, G, x_loaded[1])

            def turn(it, first, last):
                for s in range(N_RAW):
                    chunk = it * PER_ITER + s * CHUNKS_PER_GROUP
                    if not last:
                        sp.wait_ge(turned, chunk + CHUNKS_PER_GROUP)
                        load_x(s, (chunk + PER_ITER) * T, 0, G, x_loaded[s])
                    if not (first and s == 0):
                        sp.wait_ge(evacuated, chunk)
                        store((2 * s - 1) % N_STORE, (chunk - 2) * T)
                    sp.wait_ge(evacuated, chunk + 2)
                    store(2 * s, chunk * T)

            turn(0, True, False)
            with sp.Fori(1, ITERS - 1) as it:
                turn(it, False, False)
            turn(ITERS - 1, False, True)
            sp.wait_ge(evacuated, CHUNKS)
            store(N_STORE - 1, (CHUNKS - 2) * T)
            for s in range(N_STORE):
                sp.wait_ge(stored[s], 16 * (CHUNKS // (2 * N_STORE)))

        @block.gpsimd
        def _(pool):
            pool.memset(ident[:, :], 0.0).then_inc(ident_zeroed, 1)
            pool.wait_ge(ident_zeroed, 1)
            pool.affine_select(out=ident[:, :], in_=ident[:, :], compare_op=ALU.not_equal, fill=1.0,
                               base=0, pattern=[[-1, P]], channel_multiplier=1).then_inc(ident_ready, 1)

            def lo(chunk, s, first):
                pool.wait_ge(hi_ready, chunk + 1)
                if not first:
                    pool.wait_ge(multiplied, chunk - N_SPLIT + 1)
                pool.tensor_tensor(x_lo[s][:, :, :, :], x_t[s][:, :, :, :], x_hi[s][:, :, :, :].bitcast(F32),
                                   ALU.subtract).then_inc(lo_ready, 1)

            for c in range(N_SPLIT):
                lo(c, c, True)
            for c in range(N_SPLIT, PER_ITER):
                lo(c, c % N_SPLIT, False)
            with pool.Fori(1, ITERS) as it:
                for c in range(PER_ITER):
                    lo(it * PER_ITER + c, c % N_SPLIT, False)

        @block.scalar
        def _(act):
            for q in range(NQ):
                act.dma_start(w_e[Q * q:Q * (q + 1), 0:NJ * C].rearrange("p (j c) -> p j c", j=NJ),
                              w_e_dram[q]).then_inc(w_e_loaded, 16)
            act.dma_start(b_proj_sb[:, :], b_proj_dram).then_inc(b_proj_loaded, 16)

            def hi(chunk, s, first):
                act.wait_ge(turned, chunk + 1)
                if not first:
                    act.wait_ge(multiplied, chunk - N_SPLIT + 1)
                act.copy(x_hi[s][:, :, :, :], x_t[s][:, :, :, :]).then_inc(hi_ready, 1)

            act.wait_ge(w_diag_ready, NQ)
            for j in range(NJ):
                act.copy(w_hi[:, j, :], w_e[:, j * C:(j + 1) * C]).then_inc(w_hi_ready, 1)
            hi(0, 0, True)
            act.wait_ge(h_ready, 1)
            act.wait_ge(b_proj_loaded, 16)
            for e in range(NJ):
                last = act.activation(u_t[:, e, :], h_psum[:, e, :], ACT.Gelu, bias=b_proj_sb[:, e:e + 1])
            last.then_inc(u_ready, 1)
            for c in range(1, N_SPLIT):
                hi(c, c, True)
            for c in range(N_SPLIT, PER_ITER):
                hi(c, c % N_SPLIT, False)
            with act.Fori(1, ITERS) as it:
                for c in range(PER_ITER):
                    hi(it * PER_ITER + c, c % N_SPLIT, False)

        @block.vector
        def _(dve):
            def transpose(chunk, c, first):
                s = c % N_SPLIT
                group, at = divmod(c, CHUNKS_PER_GROUP)
                if not first:
                    dve.wait_ge(lo_ready, chunk - N_SPLIT + 1)
                dve.transpose(
                    x_t[s][:, :, :, :].rearrange("p t j (m i) -> p m (t j) i", m=NM),
                    x_raw[group][:, :, at * T:(at + 1) * T, :].rearrange("p m t (j k) -> p m (t j) k", k=Q),
                ).then_inc(turned, 1)

            def evacuate(it, c, first):
                dve.wait_ge(multiplied, it * PER_ITER + c + 1)
                if c % 2 == 0 and not first:
                    dve.wait_ge(stored[c // 2 % N_STORE], 16 * it)
                dve.tensor_tensor(y[c // 2 % N_STORE][:, c % 2, :, :], banks[c % N_BANKS][:, :, :],
                                  bias[:, :, :], ALU.add).then_inc(evacuated, 1)

            dve.wait_ge(cond_loaded, 16 * NQ)
            dve.transpose(cond_t[:, :, :].rearrange("p j (m i) -> p m j i", m=NM),
                          cond_raw[:, :, :].rearrange("p m (j k) -> p m j k", k=Q)).then_inc(cond_turned, 1)
            dve.wait_ge(w_e_loaded, 16 * NQ)
            dve.wait_ge(ident_ready, 1)
            for q in range(NQ):
                quad = slice(Q * q, Q * (q + 1))
                diag = w_e[quad, P * q:P * q + NJ * (C + Q)].rearrange("p (j w) -> p j w", j=NJ)[:, :, 0:Q]
                dve.tensor_tensor(diag, diag, ident[quad, quad].unsqueeze(1).to_broadcast([Q, NJ, Q]),
                                  ALU.add).then_inc(w_diag_ready, 1)
            dve.wait_ge(first_x_loaded, LOADS)
            transpose(0, 0, True)
            for j in range(NJ):
                dve.wait_ge(w_hi_ready, j + 1)
                dve.tensor_tensor(w_lo[:, j, :], w_e[:, j * C:(j + 1) * C], w_hi[:, j, :].bitcast(F32),
                                  ALU.subtract).then_inc(w_lo_ready, 1)
            dve.wait_ge(x_loaded[0], LOADS)
            transpose(1, 1, True)
            transpose(2, 2, True)
            dve.wait_ge(bias_summed, 1)
            for t in range(T):
                dve.tensor_copy(bias[:, t, :], bias_psum).then_inc(bias_ready, 1)
            dve.wait_ge(bias_ready, T)

            def turn(it, first, last):
                base = it * PER_ITER
                for c in range(PER_ITER):
                    ahead = c + LEAD
                    if not (last and ahead >= PER_ITER):
                        if ahead % CHUNKS_PER_GROUP == 0:
                            dve.wait_ge(x_loaded[ahead // CHUNKS_PER_GROUP % N_RAW],
                                        (it + 1 + ahead // PER_ITER) * LOADS)
                        transpose(base + ahead, ahead % PER_ITER, first and ahead < N_SPLIT)
                    evacuate(it, c, first)

            turn(0, True, False)
            with dve.Fori(1, ITERS - 1) as it:
                turn(it, False, False)
            turn(ITERS - 1, False, True)

        @block.tensor
        def _(pe):
            pe.wait_ge(cond_turned, 1)
            pe.wait_ge(w_proj_loaded, 16 * NQ)
            w_proj_cols = w_proj_sb[:, :, :].rearrange("p j (d e) -> p j e d", e=NJ)
            for e in range(NJ):
                for j in range(NJ):
                    last = pe.matmul(h_psum[:, e, :], w_proj_cols[:, j, e, :], cond_t[:, j, :],
                                     start=(j == 0), stop=(j == NJ - 1))
            last.then_inc(h_ready, 1)

            def products(chunk, c, first):
                s = c % N_SPLIT
                pe.wait_ge(lo_ready, chunk + 1)
                if not first:
                    pe.wait_ge(evacuated, chunk - N_BANKS + 1)
                for t in range(T):
                    for j in range(NJ):
                        pe.matmul(banks[s][:, t, :], x_hi[s][:, t, j, :], w_hi[:, j, :], start=(j == 0), stop=False)
                        pe.matmul(banks[s][:, t, :], x_hi[s][:, t, j, :], w_lo[:, j, :], start=False, stop=False)
                        last = pe.matmul(banks[s][:, t, :], x_lo[s][:, t, j, :], w_hi[:, j, :], start=False,
                                         stop=(j == NJ - 1))
                last.then_inc(multiplied, 1)

            pe.wait_ge(w_lo_ready, NJ)
            products(0, 0, True)
            pe.wait_ge(u_ready, 1)
            pe.wait_ge(w_u_loaded, 16)
            for e in range(NJ):
                last = pe.matmul(bias_psum, u_t[:, e, :], w_u[:, e, :], start=(e == 0), stop=(e == NJ - 1))
            last.then_inc(bias_summed, 1)
            products(1, 1, True)
            products(2, 2, True)
            pe.wait_ge(bias_ready, T)
            products(3, 3, True)
            for c in range(N_SPLIT, PER_ITER):
                products(c, c, False)
            with pe.Fori(1, ITERS) as it:
                for c in range(PER_ITER):
                    products(it * PER_ITER + c, c, False)


_INS = ["x", "cond_1024", "L0_cond_weight_matrix", "L0_cond_W_proj", "L0_cond_b_proj"]


def kernel(**inputs):
    import numpy as np
    import concourse.bacc as bacc
    from concourse.bass_utils import run_bass_kernel_spmd

    nc = bacc.Bacc("TRN2", target_bir_lowering=False, num_devices=1)
    arrays, args = {}, []
    for name in _INS:
        a = np.ascontiguousarray(inputs[name])
        arrays[f"in_{name}"] = a
        args.append(nc.dram_tensor(f"in_{name}", a.shape, mybir.dt.from_np(a.dtype), kind="ExternalInput").ap())
    out = nc.dram_tensor("out", inputs["x"].shape, F32, kind="ExternalOutput").ap()
    build_cond_residual(nc, *args, out)
    result = run_bass_kernel_spmd(nc, [arrays], core_ids=[0])
    return result.results[0]["out"]
```

```python
from contextlib import ExitStack

import concourse.bass as bass
from concourse import mybir

F32 = mybir.dt.float32
F32R = mybir.dt.float32r
BF16 = mybir.dt.bfloat16
ALU = mybir.AluOpType
ACT = mybir.ActivationFunctionType

P = 128
Q = 32
NQ = P // Q
TILES_PER_CHUNK = 2
CHUNKS_PER_GROUP = 4
N_RAW = 2
N_SPLIT = 4
N_BANKS = 4
N_STORE = 4
LEAD = 3
WARM_UP = 10


def build_cond_residual(nc, x, cond, weight_matrix, w_proj, b_proj, out):
    B, N, D = x.shape
    C = weight_matrix.shape[1]
    assert B == P and D == C == 4 * P
    NJ = D // P
    NM = B // Q
    T = TILES_PER_CHUNK
    G = CHUNKS_PER_GROUP * T
    TILE = NM * P
    CHUNKS = N // T
    PER_TURN = N_RAW * CHUNKS_PER_GROUP
    TURNS = CHUNKS // PER_TURN
    FIRST_BLOCKS = [1, 1, T, G - 2 * T]
    assert T == 2 and PER_TURN % N_SPLIT == 0 and PER_TURN == 2 * N_STORE and N_BANKS == N_SPLIT

    w_u_dram = weight_matrix[0:D, :].rearrange("(p j) c -> p j c", j=NJ)
    w_e_dram = weight_matrix[D:2 * D, :].rearrange("(p j) c -> p j c", j=NJ)
    w_proj_dram = w_proj.rearrange("(p j) c -> p j c", j=NJ)
    b_proj_dram = b_proj.rearrange("(p j) -> p j", j=NJ)
    cond_dram = cond.rearrange("(i m) (q w) -> q i m w", m=NM, q=NQ)
    x_dram = x.rearrange("(i m) n (q w) -> q i m n w", m=NM, q=NQ)

    with ExitStack() as ctx:
        def sb(name, shape, dt=F32):
            return ctx.enter_context(nc.sbuf_tensor(name, shape, dt))

        def sem(name):
            return ctx.enter_context(nc.semaphore(name))

        x_raw = [sb(f"x_raw{s}", [P, G * TILE]) for s in range(N_RAW)]
        x_t = [sb(f"x_t{s}", [P, T, NJ, B]) for s in range(N_SPLIT)]
        x_hi = [sb(f"x_hi{s}", [P, T, NJ, B], F32R) for s in range(N_SPLIT)]
        x_lo = [sb(f"x_lo{s}", [P, T, NJ, B], F32R) for s in range(N_SPLIT)]
        y = [sb(f"y{s}", [P, 2 * T, C]) for s in range(N_STORE)]
        w_e = sb("w_e", [P, NJ, C])
        w_hi = sb("w_hi", [P, NJ, C], F32R)
        w_lo = sb("w_lo", [P, NJ, C], F32R)
        w_proj_sb = sb("w_proj_sb", [P, NJ, C])
        w_u = sb("w_u", [P, NJ, C])
        b_proj_sb = sb("b_proj_sb", [P, NJ])
        cond_raw = sb("cond_raw", [P, NM, P])
        cond_t = sb("cond_t", [P, NJ, B])
        u_t = sb("u_t", [P, NJ, B])
        bias = sb("bias", [P, T, C])
        ident = sb("ident", [P, P])
        zeros = sb("zeros", [P, C], BF16)

        banks = [ctx.enter_context(nc.psum_tensor(f"banks{s}", [P, T, C], F32)) for s in range(N_BANKS)]
        h_psum = banks[N_BANKS - 1][:, 0, :].rearrange("p (e b) -> p e b", e=NJ)
        bias_psum = banks[N_BANKS - 1][:, 1, :]

        cond_loaded = sem("cond_loaded")
        w_proj_loaded = sem("w_proj_loaded")
        b_proj_loaded = sem("b_proj_loaded")
        w_e_loaded = [sem(f"w_e_loaded{j}") for j in range(NJ)]
        w_u_loaded = sem("w_u_loaded")
        first_blocks_loaded = [sem(f"first_blocks_loaded{n}") for n in range(len(FIRST_BLOCKS))]
        x_loaded = [sem(f"x_loaded{s}") for s in range(N_RAW)]
        zeros_ready = sem("zeros_ready")
        ident_zeroed = sem("ident_zeroed")
        ident_ready = sem("ident_ready")
        cond_turned = sem("cond_turned")
        h_ready = sem("h_ready")
        u_ready = sem("u_ready")
        bias_summed = sem("bias_summed")
        bias_ready = sem("bias_ready")
        w_diag_ready = sem("w_diag_ready")
        w_hi_ready = sem("w_hi_ready")
        w_lo_ready = sem("w_lo_ready")
        first_turned = sem("first_turned")
        first_hi_ready = sem("first_hi_ready")
        first_lo_ready = sem("first_lo_ready")
        turned = sem("turned")
        hi_ready = sem("hi_ready")
        lo_ready = sem("lo_ready")
        multiplied = sem("multiplied")
        last_multiplied = sem("last_multiplied")
        evacuated = sem("evacuated")
        last_evacuated = sem("last_evacuated")
        stored = [sem(f"stored{s}") for s in range(N_STORE)]
        last_stored = sem("last_stored")

        block = ctx.enter_context(nc.Block())

        LOADS = NQ * 16

        def raw_block(slot, tile, count):
            return x_raw[slot][:, tile * TILE:(tile + count) * TILE].rearrange(
                "p (m n w) -> p m n w", m=NM, n=count)

        @block.sync
        def _(sp):
            def load_x(slot, n, tile, count, loaded):
                for q in range(NQ):
                    sp.dma_start(raw_block(slot, tile, count)[Q * q:Q * (q + 1)],
                                 x_dram[q, :, :, bass.ds(n, count), :]).then_inc(loaded, 16)

            def store(slot, n):
                sp.dma_start(out[:, bass.ds(n, 2 * T), :], y[slot][:, :, :]).then_inc(stored[slot], 16)

            tile = 0
            for n, count in enumerate(FIRST_BLOCKS):
                load_x(0, tile, tile, count, first_blocks_loaded[n])
                tile += count
                if n == 1:
                    for q in range(NQ):
                        sp.dma_start(cond_raw[Q * q:Q * (q + 1), :, :], cond_dram[q]).then_inc(cond_loaded, 16)
                    sp.dma_start(w_proj_sb[:, :, :], w_proj_dram).then_inc(w_proj_loaded, 16)
                    sp.dma_start(b_proj_sb[:, :], b_proj_dram).then_inc(b_proj_loaded, 16)
                if n == 2:
                    sp.dma_start(w_u[:, :, :], w_u_dram).then_inc(w_u_loaded, 16)
            load_x(1, G, 0, G, x_loaded[1])

            def turn(it, first, last):
                for s in range(N_RAW):
                    chunk = it * PER_TURN + s * CHUNKS_PER_GROUP
                    if not last:
                        sp.wait_ge(turned, chunk + CHUNKS_PER_GROUP - 1)
                        load_x(s, (chunk + PER_TURN) * T, 0, G, x_loaded[s])
                    if not (first and s == 0):
                        sp.wait_ge(evacuated, chunk)
                        store((2 * s - 1) % N_STORE, (chunk - 2) * T)
                    sp.wait_ge(evacuated, chunk + 2)
                    store(2 * s, chunk * T)

            turn(0, True, False)
            with sp.Fori(1, TURNS - 1) as it:
                turn(it, False, False)
            turn(TURNS - 1, False, True)
            sp.wait_ge(evacuated, CHUNKS - 1)
            sp.dma_start(out[:, N - 2 * T:N - T, :], y[N_STORE - 1][:, 0:T, :]).then_inc(last_stored, 16)
            for t in range(T):
                sp.wait_ge(last_evacuated, t + 1)
                sp.dma_start(out[:, N - T + t, :], y[N_STORE - 1][:, T + t, :]).then_inc(last_stored, 16)
            for s in range(N_STORE - 1):
                sp.wait_ge(stored[s], 16 * TURNS)
            sp.wait_ge(stored[N_STORE - 1], 16 * (TURNS - 1))
            sp.wait_ge(last_stored, 16 * (T + 1))

        @block.gpsimd
        def _(pool):
            pool.memset(ident[:, :], 0.0).then_inc(ident_zeroed, 1)
            pool.wait_ge(ident_zeroed, 1)
            pool.affine_select(out=ident[:, :], in_=ident[:, :], compare_op=ALU.not_equal, fill=1.0,
                               base=0, pattern=[[-1, P]], channel_multiplier=1).then_inc(ident_ready, 1)

            for t in range(T):
                pool.wait_ge(first_hi_ready, t + 1)
                pool.tensor_tensor(x_lo[0][:, t, :, :], x_t[0][:, t, :, :], x_hi[0][:, t, :, :].bitcast(F32),
                                   ALU.subtract).then_inc(first_lo_ready, 1)

            def lo(chunk, s, first):
                pool.wait_ge(hi_ready, chunk)
                if not first:
                    pool.wait_ge(multiplied, chunk - N_SPLIT + 1)
                pool.tensor_tensor(x_lo[s][:, :, :, :], x_t[s][:, :, :, :], x_hi[s][:, :, :, :].bitcast(F32),
                                   ALU.subtract).then_inc(lo_ready, 1)

            for c in range(1, N_SPLIT):
                lo(c, c, True)
            with pool.Fori(1, CHUNKS // N_SPLIT) as it:
                for s in range(N_SPLIT):
                    lo(it * N_SPLIT + s, s, False)

        @block.scalar
        def _(act):
            for j in range(NJ):
                act.dma_start(w_e[:, j, :], w_e_dram[:, j, :]).then_inc(w_e_loaded[j], 16)

            for t in range(T):
                act.wait_ge(first_turned, t + 1)
                act.copy(x_hi[0][:, t, :, :], x_t[0][:, t, :, :]).then_inc(first_hi_ready, 1)

            def hi(chunk, s, first):
                act.wait_ge(turned, chunk)
                if not first:
                    act.wait_ge(multiplied, chunk - N_SPLIT + 1)
                act.copy(x_hi[s][:, :, :, :], x_t[s][:, :, :, :]).then_inc(hi_ready, 1)

            hi(1, 1, True)
            act.wait_ge(h_ready, 1)
            act.wait_ge(b_proj_loaded, 16)
            for e in range(NJ):
                last = act.activation(u_t[:, e, :], h_psum[:, e, :], ACT.Gelu, bias=b_proj_sb[:, e:e + 1])
            last.then_inc(u_ready, 1)
            for c in range(2, N_SPLIT):
                hi(c, c, True)
            with act.Fori(1, CHUNKS // N_SPLIT) as it:
                for s in range(N_SPLIT):
                    hi(it * N_SPLIT + s, s, False)

        @block.vector
        def _(dve):
            def transpose(out_, in_):
                return dve.transpose(out_.rearrange("p j (i m) -> p m j i", m=NM),
                                     in_.rearrange("p m (k j) -> p m j k", k=Q))

            def transpose_chunk(chunk, c, raw, first):
                if not first:
                    dve.wait_ge(lo_ready, chunk - N_SPLIT)
                for t in range(T):
                    last = transpose(x_t[c % N_SPLIT][:, t, :, :], raw[:, :, t, :])
                last.then_inc(turned, 1)

            def evacuate(it, c, first):
                dve.wait_ge(multiplied, it * PER_TURN + c + 1)
                if c % 2 == 0 and not first:
                    dve.wait_ge(stored[c // 2], 16 * it)
                dve.tensor_tensor(y[c // 2][:, c % 2 * T:(c % 2 + 1) * T, :], banks[c % N_BANKS][:, :, :],
                                  bias[:, :, :], ALU.add).then_inc(evacuated, 1)

            dve.memset(zeros[:, :], 0.0).then_inc(zeros_ready, 1)

            def w_diag(j):
                dve.wait_ge(w_e_loaded[j], 16)
                diag = w_e[:, j, :].rearrange("p (a r) -> p a r", r=NJ)[:, :, j]
                dve.tensor_tensor(diag, diag, ident[:, :], ALU.add).then_inc(w_diag_ready, 1)
                dve.wait_ge(w_diag_ready, j + 1)
                dve.tensor_copy(w_hi[:, j, :], w_e[:, j, :]).then_inc(w_hi_ready, 1)

            for t in range(T):
                dve.wait_ge(first_blocks_loaded[t], LOADS)
                transpose(x_t[0][:, t, :, :], raw_block(0, t, 1)[:, :, 0, :]).then_inc(first_turned, 1)
                if t == 0:
                    dve.wait_ge(ident_ready, 1)
                    for j in range(NJ):
                        w_diag(j)
            for j in range(NJ):
                dve.wait_ge(w_hi_ready, j + 1)
                dve.tensor_tensor(w_lo[:, j, :], w_e[:, j, :], w_hi[:, j, :].bitcast(F32),
                                  ALU.subtract).then_inc(w_lo_ready, 1)
            dve.wait_ge(cond_loaded, LOADS)
            transpose(cond_t[:, :, :], cond_raw[:, :, :]).then_inc(cond_turned, 1)
            dve.wait_ge(first_blocks_loaded[2], LOADS)
            transpose_chunk(1, 1, raw_block(0, T, T), True)
            dve.wait_ge(first_blocks_loaded[3], LOADS)
            rest = raw_block(0, 2 * T, G - 2 * T)
            transpose_chunk(2, 2, rest[:, :, 0:T, :], True)
            dve.wait_ge(bias_summed, 1)
            for t in range(T):
                dve.tensor_copy(bias[:, t, :], bias_psum).then_inc(bias_ready, 1)
            dve.wait_ge(bias_ready, T)

            def turn(it, first, last):
                for c in range(PER_TURN):
                    ahead = c + LEAD
                    if not (last and ahead >= PER_TURN):
                        group, at = divmod(ahead % PER_TURN, CHUNKS_PER_GROUP)
                        if at == 0:
                            dve.wait_ge(x_loaded[group], (it + 1) * LOADS)
                        raw = raw_block(group, 0, G)[:, :, at * T:(at + 1) * T, :]
                        if first and ahead == 3:
                            raw = rest[:, :, T:2 * T, :]
                        transpose_chunk(it * PER_TURN + ahead, ahead % PER_TURN, raw, first and ahead < N_SPLIT)
                    if not (last and c == PER_TURN - 1):
                        evacuate(it, c, first)

            turn(0, True, False)
            with dve.Fori(1, TURNS - 1) as it:
                turn(it, False, False)
            turn(TURNS - 1, False, True)
            for t in range(T):
                dve.wait_ge(last_multiplied, t + 1)
                dve.tensor_tensor(y[N_STORE - 1][:, T + t, :], banks[N_BANKS - 1][:, t, :], bias[:, t, :],
                                  ALU.add).then_inc(last_evacuated, 1)

        @block.tensor
        def _(pe):
            pe.wait_ge(zeros_ready, 1)
            for _ in range(WARM_UP):
                pe.matmul(bias_psum, zeros[:, 0:P], zeros[:, :], start=True, stop=True)

            def product(bank, a, b, j, first=False, last=False):
                return pe.matmul(bank, a[:, j, :], b[:, j, :], start=first, stop=last)

            for t in range(T):
                pe.wait_ge(first_hi_ready, t + 1)
                for j in range(NJ):
                    if t == 0:
                        pe.wait_ge(w_hi_ready, j + 1)
                    product(banks[0][:, t, :], x_hi[0][:, t], w_hi, j, first=(j == 0))
            for t in range(T):
                pe.wait_ge(first_lo_ready, t + 1)
                for j in range(NJ):
                    product(banks[0][:, t, :], x_lo[0][:, t], w_hi, j)
            for t in range(T):
                for j in range(NJ):
                    if t == 0:
                        pe.wait_ge(w_lo_ready, j + 1)
                    last = product(banks[0][:, t, :], x_hi[0][:, t], w_lo, j, last=(j == NJ - 1))
            last.then_inc(multiplied, 1)

            pe.wait_ge(cond_turned, 1)
            pe.wait_ge(w_proj_loaded, 16)
            w_proj_cols = w_proj_sb[:, :, :].rearrange("p j (d e) -> p j e d", e=NJ)
            for e in range(NJ):
                for j in range(NJ):
                    last = pe.matmul(h_psum[:, e, :], w_proj_cols[:, j, e, :], cond_t[:, j, :],
                                     start=(j == 0), stop=(j == NJ - 1))
            last.then_inc(h_ready, 1)

            def products(chunk, s, first, by_tile=False):
                pe.wait_ge(lo_ready, chunk)
                if not first:
                    pe.wait_ge(evacuated, chunk - N_BANKS + 1)
                for t in range(T):
                    for j in range(NJ):
                        product(banks[s][:, t, :], x_hi[s][:, t], w_hi, j, first=(j == 0))
                        product(banks[s][:, t, :], x_hi[s][:, t], w_lo, j)
                        last = product(banks[s][:, t, :], x_lo[s][:, t], w_hi, j, last=(j == NJ - 1))
                    if by_tile:
                        last.then_inc(last_multiplied, 1)
                if not by_tile:
                    last.then_inc(multiplied, 1)

            products(1, 1, True)
            pe.wait_ge(u_ready, 1)
            pe.wait_ge(w_u_loaded, 16)
            for e in range(NJ):
                last = pe.matmul(bias_psum, u_t[:, e, :], w_u[:, e, :], start=(e == 0), stop=(e == NJ - 1))
            last.then_inc(bias_summed, 1)
            products(2, 2, True)
            pe.wait_ge(bias_ready, T)
            products(3, 3, True)
            with pe.Fori(1, CHUNKS // N_SPLIT - 1) as it:
                for s in range(N_SPLIT):
                    products(it * N_SPLIT + s, s, False)
            for c in range(CHUNKS - N_SPLIT, CHUNKS):
                products(c, c % N_SPLIT, False, by_tile=(c == CHUNKS - 1))


_INS = ["x", "cond_1024", "L0_cond_weight_matrix", "L0_cond_W_proj", "L0_cond_b_proj"]


def kernel(**inputs):
    import numpy as np
    import concourse.bacc as bacc
    from concourse.bass_utils import run_bass_kernel_spmd

    nc = bacc.Bacc("TRN2", target_bir_lowering=False, num_devices=1)
    arrays, args = {}, []
    for name in _INS:
        a = np.ascontiguousarray(inputs[name])
        arrays[f"in_{name}"] = a
        args.append(nc.dram_tensor(f"in_{name}", a.shape, mybir.dt.from_np(a.dtype), kind="ExternalInput").ap())
    out = nc.dram_tensor("out", inputs["x"].shape, F32, kind="ExternalOutput").ap()
    build_cond_residual(nc, *args, out)
    result = run_bass_kernel_spmd(nc, [arrays], core_ids=[0])
    return result.results[0]["out"]
```

```python
from contextlib import ExitStack

import concourse.bass as bass
from concourse import mybir

F32 = mybir.dt.float32
F32R = mybir.dt.float32r
BF16 = mybir.dt.bfloat16
ALU = mybir.AluOpType
ACT = mybir.ActivationFunctionType

P = 128
Q = 32
NQ = P // Q
TILES_PER_CHUNK = 2
CHUNKS_PER_GROUP = 4
N_RAW = 2
N_SPLIT = 4
N_BANKS = 4
N_STORE = 4
LEAD = 4
DIRECT = 2
WARM_UP = 5


def build_cond_residual(nc, x, cond, weight_matrix, w_proj, b_proj, out):
    B, N, D = x.shape
    C = weight_matrix.shape[1]
    assert B == P and D == C == 4 * P
    NJ = D // P
    NM = B // Q
    T = TILES_PER_CHUNK
    G = CHUNKS_PER_GROUP * T
    TILE = NM * P
    CHUNKS = N // T
    PER_TURN = N_RAW * CHUNKS_PER_GROUP
    TURNS = CHUNKS // PER_TURN
    assert T == 2 and PER_TURN % N_SPLIT == 0 and PER_TURN == 2 * N_STORE and N_BANKS == N_SPLIT
    PIECES = [(t, slice(0, C)) for t in range(T - 1)] + [(T - 1, slice(0, C // 2)), (T - 1, slice(C // 2, C))]
    assert DIRECT == 2 and N_BANKS >= DIRECT + 2

    w_u_dram = weight_matrix[0:D, :].rearrange("(p j) c -> p j c", j=NJ)
    w_e_dram = weight_matrix[D:2 * D, :].rearrange("(p j) c -> p j c", j=NJ)
    w_proj_dram = w_proj.rearrange("(p j) c -> p j c", j=NJ)
    b_proj_dram = b_proj.rearrange("(p j) -> p j", j=NJ)
    x_dram = x.rearrange("(i m) n (q w) -> q i m n w", m=NM, q=NQ)

    with ExitStack() as ctx:
        def sb(name, shape, dt=F32):
            return ctx.enter_context(nc.sbuf_tensor(name, shape, dt))

        def sem(name):
            return ctx.enter_context(nc.semaphore(name))

        x_raw = [sb(f"x_raw{s}", [P, G * TILE]) for s in range(N_RAW)]
        x_t = [sb(f"x_t{s}", [P, T, NJ, B]) for s in range(N_SPLIT)]
        x_hi = [sb(f"x_hi{s}", [P, T, NJ, B], F32R) for s in range(N_SPLIT)]
        x_lo = [sb(f"x_lo{s}", [P, T, NJ, B], F32R) for s in range(N_SPLIT)]
        y = [sb(f"y{s}", [P, 2 * T, C]) for s in range(N_STORE)]
        w_e = sb("w_e", [P, NJ, C])
        w_hi = sb("w_hi", [P, NJ, C], F32R)
        w_lo = sb("w_lo", [P, NJ, C], F32R)
        w_proj_sb = sb("w_proj_sb", [P, NJ, C])
        w_u = sb("w_u", [P, NJ, C])
        b_proj_sb = sb("b_proj_sb", [P, NJ])
        cond_sb = sb("cond_sb", [B, D])
        cond_t = sb("cond_t", [P, NJ, B])
        w_u_hi = sb("w_u_hi", [P, NJ, C], F32R)
        w_u_lo = sb("w_u_lo", [P, NJ, C], F32R)
        u_t = sb("u_t", [P, NJ, B])
        u_hi = sb("u_hi", [P, NJ, B], F32R)
        u_lo = sb("u_lo", [P, NJ, B], F32R)
        bias = sb("bias", [P, C])
        ident = sb("ident", [P, P])
        zeros = sb("zeros", [P, C], BF16)
        scratch = sb("scratch", [P, 1])

        banks = [ctx.enter_context(nc.psum_tensor(f"banks{s}", [P, T, C], F32)) for s in range(N_BANKS)]
        piece_psum = [banks[N_BANKS - 1][:, t, cols] for t, cols in PIECES[:T]] + [banks[0][:, 0, PIECES[T][1]]]
        direct_psum = [banks[DIRECT][:, t, :].rearrange("p (j b) -> p j b", j=NJ) for t in range(T)]
        cond_psum = banks[N_BANKS - 1][:, 1, :].rearrange("p (j b) -> p j b", j=NJ)
        h_psum = banks[N_BANKS - 1][:, 0, :].rearrange("p (e b) -> p e b", e=NJ)
        bias_psum = banks[N_BANKS - 1][:, 1, :]

        cond_loaded = sem("cond_loaded")
        w_proj_loaded = sem("w_proj_loaded")
        b_proj_loaded = sem("b_proj_loaded")
        w_e_loaded = [sem(f"w_e_loaded{j}") for j in range(NJ)]
        w_u_loaded = sem("w_u_loaded")
        direct_loaded = [sem(f"direct_loaded{n}") for n in range(3)]
        first_blocks_loaded = [sem(f"first_blocks_loaded{n}") for n in range(2)]
        x_loaded = [sem(f"x_loaded{s}") for s in range(N_RAW)]
        zeros_ready = sem("zeros_ready")
        scratch_written = sem("scratch_written")
        ident_zeroed = sem("ident_zeroed")
        ident_ready = sem("ident_ready")
        cond_flipped = sem("cond_flipped")
        cond_ready = sem("cond_ready")
        h_ready = sem("h_ready")
        u_ready = sem("u_ready")
        u_hi_ready = sem("u_hi_ready")
        u_lo_ready = sem("u_lo_ready")
        w_u_hi_ready = sem("w_u_hi_ready")
        w_u_lo_ready = sem("w_u_lo_ready")
        bias_summed = sem("bias_summed")
        bias_ready = sem("bias_ready")
        w_diag_ready = sem("w_diag_ready")
        w_hi_ready = [sem(f"w_hi_ready{j}") for j in range(NJ)]
        w_lo_ready = [sem(f"w_lo_ready{j}") for j in range(NJ)]
        direct_flipped = sem("direct_flipped")
        direct_hi_ready = sem("direct_hi_ready")
        direct_lo_ready = sem("direct_lo_ready")
        turned = sem("turned")
        hi_ready = sem("hi_ready")
        lo_ready = sem("lo_ready")
        multiplied = sem("multiplied")
        last_multiplied = sem("last_multiplied")
        evacuated = sem("evacuated")
        last_evacuated = sem("last_evacuated")
        stored = [sem(f"stored{s}") for s in range(N_STORE)]
        last_stored = sem("last_stored")

        block = ctx.enter_context(nc.Block())

        LOADS = NQ * 16

        def raw_block(slot, tile, count):
            return x_raw[slot][:, tile * TILE:(tile + count) * TILE].rearrange(
                "p (m n w) -> p m n w", m=NM, n=count)

        direct = x_raw[0][:, 0:DIRECT * T * TILE].rearrange("p (n d) -> p n d", n=DIRECT * T)

        @block.sync
        def _(sp):
            def load_x(slot, n, tile, count, loaded):
                for q in range(NQ):
                    sp.dma_start(raw_block(slot, tile, count)[Q * q:Q * (q + 1)],
                                 x_dram[q, :, :, bass.ds(n, count), :]).then_inc(loaded, 16)

            def store(slot, n):
                sp.dma_start(out[:, bass.ds(n, 2 * T), :], y[slot][:, :, :]).then_inc(stored[slot], 16)

            def load_direct(n, tile, count):
                sp.dma_start(direct[:, tile:tile + count, :], x[:, tile:tile + count, :]).then_inc(direct_loaded[n], 16)

            def load_w_e(j):
                sp.dma_start(w_e[:, j, :], w_e_dram[:, j, :]).then_inc(w_e_loaded[j], 16)

            load_direct(0, 0, 1)
            load_direct(1, 1, 1)
            for j in range(NJ):
                load_w_e(j)
            load_direct(2, T, T)
            sp.dma_start(cond_sb[:, :], cond).then_inc(cond_loaded, 16)
            sp.dma_start(w_proj_sb[:, :, :], w_proj_dram).then_inc(w_proj_loaded, 16)
            sp.dma_start(b_proj_sb[:, :], b_proj_dram).then_inc(b_proj_loaded, 16)
            load_x(0, DIRECT * T, DIRECT * T, T, first_blocks_loaded[0])
            sp.dma_start(w_u[:, :, :], w_u_dram).then_inc(w_u_loaded, 16)
            load_x(0, (DIRECT + 1) * T, (DIRECT + 1) * T, T, first_blocks_loaded[1])
            load_x(1, G, 0, G, x_loaded[1])

            def turn(it, first, last):
                for s in range(N_RAW):
                    chunk = it * PER_TURN + s * CHUNKS_PER_GROUP
                    if not last:
                        sp.wait_ge(turned, chunk + CHUNKS_PER_GROUP - DIRECT)
                        if first and s == 0:
                            sp.wait_ge(direct_flipped, DIRECT * T)
                        load_x(s, (chunk + PER_TURN) * T, 0, G, x_loaded[s])
                    if not (first and s == 0):
                        sp.wait_ge(evacuated, chunk)
                        store((2 * s - 1) % N_STORE, (chunk - 2) * T)
                    sp.wait_ge(evacuated, chunk + 2)
                    store(2 * s, chunk * T)

            turn(0, True, False)
            with sp.Fori(1, TURNS - 1) as it:
                turn(it, False, False)
            turn(TURNS - 1, False, True)
            sp.wait_ge(evacuated, CHUNKS - 1)
            sp.dma_start(out[:, N - 2 * T:N - T, :], y[N_STORE - 1][:, 0:T, :]).then_inc(last_stored, 16)
            for n, (t, cols) in enumerate(PIECES):
                sp.wait_ge(last_evacuated, n + 1)
                sp.dma_start(out[:, N - T + t, cols], y[N_STORE - 1][:, T + t, cols]).then_inc(last_stored, 16)
            for s in range(N_STORE - 1):
                sp.wait_ge(stored[s], 16 * TURNS)
            sp.wait_ge(stored[N_STORE - 1], 16 * (TURNS - 1))
            sp.wait_ge(last_stored, 16 * (1 + len(PIECES)))

        @block.gpsimd
        def _(pool):
            pool.memset(ident[:, :], 0.0).then_inc(ident_zeroed, 1)
            pool.wait_ge(ident_zeroed, 1)
            pool.affine_select(out=ident[:, :], in_=ident[:, :], compare_op=ALU.not_equal, fill=1.0,
                               base=0, pattern=[[-1, P]], channel_multiplier=1).then_inc(ident_ready, 1)

            pool.wait_ge(ident_ready, 1)
            for j in range(NJ):
                pool.wait_ge(w_e_loaded[j], 16)
                diag = w_e[:, j, :].rearrange("p (a r) -> p a r", r=NJ)[:, :, j]
                pool.tensor_tensor(diag, diag, ident[:, :], ALU.add).then_inc(w_diag_ready, 1)

            def lo(chunk, s, first):
                pool.wait_ge(hi_ready, chunk + 1 - DIRECT)
                if not first:
                    pool.wait_ge(multiplied, chunk - N_SPLIT + 1)
                pool.tensor_tensor(x_lo[s][:, :, :, :], x_t[s][:, :, :, :], x_hi[s][:, :, :, :].bitcast(F32),
                                   ALU.subtract).then_inc(lo_ready, 1)

            for c in range(DIRECT, N_SPLIT):
                lo(c, c, True)
            with pool.Fori(1, CHUNKS // N_SPLIT) as it:
                for s in range(N_SPLIT):
                    lo(it * N_SPLIT + s, s, False)

        @block.scalar
        def _(act):
            def direct_hi(n):
                act.wait_ge(direct_flipped, n + 1)
                act.copy(x_hi[n // T][:, n % T, :, :], direct_psum[n % T]).then_inc(direct_hi_ready, 1)

            act.wait_ge(zeros_ready, 1)
            act.copy(scratch[:, :], zeros[:, 0:1]).then_inc(scratch_written, 1)
            for n in range(T):
                direct_hi(n)
            for j in range(1, NJ):
                act.wait_ge(w_diag_ready, j + 1)
                act.copy(w_hi[:, j, :], w_e[:, j, :]).then_inc(w_hi_ready[j], 1)
            for n in range(T, DIRECT * T):
                direct_hi(n)

            def hi(chunk, s, first):
                act.wait_ge(turned, chunk + 1 - DIRECT)
                if not first:
                    act.wait_ge(multiplied, chunk - N_SPLIT + 1)
                act.copy(x_hi[s][:, :, :, :], x_t[s][:, :, :, :]).then_inc(hi_ready, 1)

            hi(2, 2, True)
            act.wait_ge(w_u_loaded, 16)
            act.copy(w_u_hi[:, :, :], w_u[:, :, :]).then_inc(w_u_hi_ready, 1)
            act.wait_ge(h_ready, 1)
            act.wait_ge(b_proj_loaded, 16)
            for e in range(NJ):
                last = act.activation(u_t[:, e, :], h_psum[:, e, :], ACT.Gelu, bias=b_proj_sb[:, e:e + 1])
            last.then_inc(u_ready, 1)
            act.wait_ge(u_ready, 1)
            act.copy(u_hi[:, :, :], u_t[:, :, :]).then_inc(u_hi_ready, 1)
            for c in range(3, N_SPLIT):
                hi(c, c, True)
            with act.Fori(1, CHUNKS // N_SPLIT) as it:
                for s in range(N_SPLIT):
                    hi(it * N_SPLIT + s, s, False)

        @block.vector
        def _(dve):
            def transpose(out_, in_):
                return dve.transpose(out_.rearrange("p j (i m) -> p m j i", m=NM),
                                     in_.rearrange("p m (k j) -> p m j k", k=Q))

            def transpose_chunk(chunk, c, raw, first):
                if not first:
                    dve.wait_ge(lo_ready, chunk - N_SPLIT + 1 - DIRECT)
                for t in range(T):
                    last = transpose(x_t[c % N_SPLIT][:, t, :, :], raw[:, :, t, :])
                last.then_inc(turned, 1)

            def evacuate(it, c, first):
                dve.wait_ge(multiplied, it * PER_TURN + c + 1)
                if c % 2 == 0 and not first:
                    dve.wait_ge(stored[c // 2], 16 * it)
                dve.tensor_tensor(y[c // 2][:, c % 2 * T:(c % 2 + 1) * T, :], banks[c % N_BANKS][:, :, :],
                                  bias[:, :].unsqueeze(1).to_broadcast([P, T, C]), ALU.add).then_inc(evacuated, 1)

            dve.memset(zeros[:, :], 0.0).then_inc(zeros_ready, 1)

            def direct_lo(n):
                dve.wait_ge(direct_hi_ready, n + 1)
                dve.tensor_tensor(x_lo[n // T][:, n % T, :, :], direct_psum[n % T],
                                  x_hi[n // T][:, n % T, :, :].bitcast(F32), ALU.subtract).then_inc(direct_lo_ready, 1)

            dve.wait_ge(w_diag_ready, 1)
            dve.tensor_copy(w_hi[:, 0, :], w_e[:, 0, :]).then_inc(w_hi_ready[0], 1)
            for n in range(T):
                direct_lo(n)
            for j in range(NJ):
                dve.wait_ge(w_hi_ready[j], 1)
                dve.tensor_tensor(w_lo[:, j, :], w_e[:, j, :], w_hi[:, j, :].bitcast(F32),
                                  ALU.subtract).then_inc(w_lo_ready[j], 1)
            for n in range(T, DIRECT * T):
                direct_lo(n)
            dve.wait_ge(cond_flipped, 1)
            dve.tensor_copy(cond_t[:, :, :], cond_psum).then_inc(cond_ready, 1)
            for c in range(DIRECT, LEAD + 1):
                if c < N_SPLIT:
                    dve.wait_ge(first_blocks_loaded[c - DIRECT], LOADS)
                    transpose_chunk(c, c, raw_block(0, c * T, T), True)
                else:
                    dve.wait_ge(w_u_hi_ready, 1)
                    dve.tensor_tensor(w_u_lo[:, :, :], w_u[:, :, :], w_u_hi[:, :, :].bitcast(F32),
                                      ALU.subtract).then_inc(w_u_lo_ready, 1)
                    dve.wait_ge(x_loaded[1], LOADS)
                    transpose_chunk(c, c, raw_block(1, 0, G)[:, :, 0:T, :], True)
            dve.wait_ge(u_hi_ready, 1)
            dve.tensor_tensor(u_lo[:, :, :], u_t[:, :, :], u_hi[:, :, :].bitcast(F32),
                              ALU.subtract).then_inc(u_lo_ready, 1)
            dve.wait_ge(bias_summed, 1)
            dve.tensor_copy(bias[:, :], bias_psum).then_inc(bias_ready, 1)
            dve.wait_ge(bias_ready, 1)

            def turn(it, first, last):
                for c in range(PER_TURN):
                    ahead = c + LEAD
                    if not (last and ahead >= PER_TURN) and not (first and ahead <= LEAD):
                        group, at = divmod(ahead % PER_TURN, CHUNKS_PER_GROUP)
                        if at == 0:
                            dve.wait_ge(x_loaded[group], (it + 1) * LOADS)
                        raw = raw_block(group, 0, G)[:, :, at * T:(at + 1) * T, :]
                        transpose_chunk(it * PER_TURN + ahead, ahead % PER_TURN, raw, first and ahead < N_SPLIT + DIRECT)
                    if not (last and c == PER_TURN - 1):
                        evacuate(it, c, first)

            turn(0, True, False)
            with dve.Fori(1, TURNS - 1) as it:
                turn(it, False, False)
            turn(TURNS - 1, False, True)
            for n, (t, cols) in enumerate(PIECES):
                dve.wait_ge(last_multiplied, n + 1)
                dve.tensor_tensor(y[N_STORE - 1][:, T + t, cols], piece_psum[n], bias[:, cols],
                                  ALU.add).then_inc(last_evacuated, 1)

        @block.tensor
        def _(pe):
            def flip(psum, rows, done):
                for j in range(NJ):
                    last = pe.transpose(psum[:, j, :], rows.rearrange("b (p j) -> b j p", j=NJ)[:, j, :], ident[:, :])
                last.then_inc(done, 1)

            pe.wait_ge(zeros_ready, 1)
            pe.wait_ge(ident_ready, 1)
            for _ in range(WARM_UP):
                pe.matmul(banks[N_BANKS - 1][:, 0, :], zeros[:, 0:P], zeros[:, :], start=True, stop=True)
            for t in range(T):
                pe.wait_ge(direct_loaded[t], 16)
                flip(direct_psum[t], direct[:, t, :], direct_flipped)

            def product(bank, a, b, j, first=False, last=False):
                return pe.matmul(bank, a[:, j, :], b[:, j, :], start=first, stop=last)

            for j in range(NJ + 1):
                if j < NJ:
                    pe.wait_ge(w_hi_ready[j], 1)
                    for t in range(T):
                        if j == 0:
                            pe.wait_ge(direct_hi_ready, t + 1)
                        product(banks[0][:, t, :], x_hi[0][:, t], w_hi, j, first=(j == 0))
                    for t in range(T):
                        if j == 0:
                            pe.wait_ge(direct_lo_ready, t + 1)
                        product(banks[0][:, t, :], x_lo[0][:, t], w_hi, j)
                if j > 0:
                    pe.wait_ge(w_lo_ready[j - 1], 1)
                    for t in range(T):
                        last = product(banks[0][:, t, :], x_hi[0][:, t], w_lo, j - 1, last=(j == NJ))
                if j == NJ - 2:
                    pe.wait_ge(direct_loaded[2], 16)
                    for t in range(T):
                        flip(direct_psum[t], direct[:, T + t, :], direct_flipped)
            last.then_inc(multiplied, 1)
            pe.wait_ge(cond_loaded, 16)
            flip(cond_psum, cond_sb[:, :], cond_flipped)

            def three_passes(bank, a_hi, a_lo, b_hi, b_lo, cols=slice(0, C)):
                for j in range(NJ):
                    pe.matmul(bank, a_hi[:, j, :], b_hi[:, j, cols], start=(j == 0), stop=False)
                    pe.matmul(bank, a_hi[:, j, :], b_lo[:, j, cols], start=False, stop=False)
                    last = pe.matmul(bank, a_lo[:, j, :], b_hi[:, j, cols], start=False, stop=(j == NJ - 1))
                return last

            def products(s):
                for t in range(T):
                    yield three_passes(banks[s][:, t, :], x_hi[s][:, t], x_lo[s][:, t], w_hi, w_lo)

            pe.wait_ge(direct_lo_ready, DIRECT * T)
            *_, last = products(1)
            last.then_inc(multiplied, 1)
            pe.wait_ge(cond_ready, 1)
            pe.wait_ge(w_proj_loaded, 16)
            w_proj_cols = w_proj_sb[:, :, :].rearrange("p j (d e) -> p j e d", e=NJ)
            for e in range(NJ):
                for j in range(NJ):
                    last = pe.matmul(h_psum[:, e, :], w_proj_cols[:, j, e, :], cond_t[:, j, :],
                                     start=(j == 0), stop=(j == NJ - 1))
            last.then_inc(h_ready, 1)

            pe.wait_ge(lo_ready, 1)
            *_, last = products(2)
            last.then_inc(multiplied, 1)

            pe.wait_ge(w_u_hi_ready, 1)
            pe.wait_ge(w_u_lo_ready, 1)
            pe.wait_ge(u_hi_ready, 1)
            pe.wait_ge(u_lo_ready, 1)
            three_passes(bias_psum, u_hi, u_lo, w_u_hi, w_u_lo).then_inc(bias_summed, 1)

            pe.wait_ge(lo_ready, 2)
            for t, last in enumerate(products(3)):
                if t == 0:
                    pe.wait_ge(bias_ready, 1)
            last.then_inc(multiplied, 1)

            with pe.Fori(1, CHUNKS // N_SPLIT - 1) as it:
                for s in range(N_SPLIT):
                    pe.wait_ge(lo_ready, it * N_SPLIT + s + 1 - DIRECT)
                    pe.wait_ge(evacuated, it * N_SPLIT + s + 1 - N_BANKS)
                    *_, last = products(s)
                    last.then_inc(multiplied, 1)
            for c in range(CHUNKS - N_SPLIT, CHUNKS - 1):
                pe.wait_ge(lo_ready, c + 1 - DIRECT)
                pe.wait_ge(evacuated, c + 1 - N_BANKS)
                *_, last = products(c % N_SPLIT)
                last.then_inc(multiplied, 1)
            pe.wait_ge(lo_ready, CHUNKS - DIRECT)
            pe.wait_ge(evacuated, CHUNKS - N_BANKS)
            s = N_SPLIT - 1
            for n, (t, cols) in enumerate(PIECES):
                if n == T:
                    pe.wait_ge(evacuated, CHUNKS - N_BANKS + 1)
                three_passes(piece_psum[n], x_hi[s][:, t], x_lo[s][:, t], w_hi, w_lo,
                             cols).then_inc(last_multiplied, 1)


_INS = ["x", "cond_1024", "L0_cond_weight_matrix", "L0_cond_W_proj", "L0_cond_b_proj"]


def kernel(**inputs):
    import numpy as np
    import concourse.bacc as bacc
    from concourse.bass_utils import run_bass_kernel_spmd

    nc = bacc.Bacc("TRN2", target_bir_lowering=False, num_devices=1)
    arrays, args = {}, []
    for name in _INS:
        a = np.ascontiguousarray(inputs[name])
        arrays[f"in_{name}"] = a
        args.append(nc.dram_tensor(f"in_{name}", a.shape, mybir.dt.from_np(a.dtype), kind="ExternalInput").ap())
    out = nc.dram_tensor("out", inputs["x"].shape, F32, kind="ExternalOutput").ap()
    build_cond_residual(nc, *args, out)
    result = run_bass_kernel_spmd(nc, [arrays], core_ids=[0])
    return result.results[0]["out"]
```
